# Optimizing a Trainium2 kernel written in Bass

```python
import numpy as np
import jax
import jax.numpy as jnp

def _softmax(x, axis=-1):
    return jax.nn.softmax(x, axis=axis)

def _gelu(x):
    return jax.nn.gelu(x, approximate=True)

def _silu(x):
    return jax.nn.silu(x)

def _sigmoid(x):
    return jax.nn.sigmoid(x)

def _layernorm(x, axis=-1, eps=1e-05):
    m = jnp.mean(x, axis=axis, keepdims=True)
    v = jnp.var(x, axis=axis, keepdims=True)
    return (x - m) / jnp.sqrt(v + eps)

def _scatter_add(tgt, idx, src, axis=0):
    return tgt.at[idx].add(src)

def _segment_sum(src, seg, n):
    return jax.ops.segment_sum(src, seg, n)
kernel_name = 'mk_cond_resid_d2_seqx_r2_6278c0'

def setup_inputs(seed: int=0):
    np.random.seed(seed)
    _w = jnp.asarray

    def _rec_inputs():
        import jax
        import jax.numpy as jnp
        _rk = jax.random.key(seed)
        x = -7.109e-05 + 0.9999 * jax.random.normal(jax.random.fold_in(_rk, 1), (32, 128, 2048), jnp.float32)
        _lenS = 128 - jax.random.randint(jax.random.fold_in(_rk, 7), (32,), 0, max(1, 128 // 4) + 1, jnp.int32)
        _lenS2 = 128 - jax.random.randint(jax.random.fold_in(_rk, 8), (32,), 0, max(1, 128 // 4) + 1, jnp.int32)
        itok_B_0_15 = jax.random.randint(jax.random.fold_in(_rk, 11), (32,), 0, 16, jnp.int32)
        itok_B_3_7 = jax.random.randint(jax.random.fold_in(_rk, 12), (32,), 3, 8, jnp.int32)
        return (x, itok_B_0_15, itok_B_3_7)
    x, itok_B_0_15, itok_B_3_7 = _rec_inputs()

    def _L0_cond_setup():
        import jax, jax.numpy as jnp
        import numpy as np
        B, C, T = (64, 128, 2048)
        S, D = (16, 128)
        key = jax.random.key(seed)
        k1, k2, k3 = jax.random.split(key, 3)
        x = jax.random.normal(k1, (B, C, T), dtype=jnp.float32)
        condition = jax.random.randint(k2, (B,), 0, S, dtype=jnp.int64)
        bound = float(np.sqrt(6.0 / C))
        weights = jax.random.uniform(k3, (S, C, D), dtype=jnp.float32, minval=-bound, maxval=bound)
        return {'x': x, 'condition': condition, 'weights': weights}
    _L0_cond_all = _L0_cond_setup()
    _L0_cond_in = {k: v for k, v in _L0_cond_all.items() if k in ('weights',)}
    del _L0_cond_all

    def _L1_cond_setup():
        import jax, jax.numpy as jnp
        import numpy as np
        MAX_LORAS, OUT, IN = (8, 2048, 2048)
        B, S = (4, 1024)
        key = jax.random.key(seed)
        k1, k2, k3 = jax.random.split(key, 3)
        x = jax.random.normal(k1, (B, S, IN), dtype=jnp.float32)
        weight = jax.random.normal(k2, (MAX_LORAS, OUT, IN), dtype=jnp.float32) * 0.02
        adapter_ids = jax.random.randint(k3, (B,), 0, MAX_LORAS, dtype=jnp.int32)
        return {'x': x, 'weight': weight, 'adapter_ids': adapter_ids}
    _L1_cond_all = _L1_cond_setup()
    _L1_cond_in = {k: v for k, v in _L1_cond_all.items() if k in ('weight',)}
    del _L1_cond_all
    return {'x': x, 'itok_B_0_15': itok_B_0_15, 'itok_B_3_7': itok_B_3_7, 'L0_cond_weights': _L0_cond_in['weights'], 'L1_cond_weight': _L1_cond_in['weight']}

def reference(x, itok_B_0_15, itok_B_3_7, L0_cond_weights, L1_cond_weight):
    import jax
    import jax.numpy as jnp

    def _L0_cond_ref(x, condition, weights):
        import jax, jax.numpy as jnp
        import numpy as np
        B, C, T = (64, 128, 2048)
        S, D = (16, 128)
        W = weights[condition]
        return jnp.einsum('bct,bcd->bdt', x, W)

    def _L1_cond_ref(x, weight, adapter_ids):
        import jax, jax.numpy as jnp
        import numpy as np
        MAX_LORAS, OUT, IN = (8, 2048, 2048)
        B, S = (4, 1024)
        w = weight[adapter_ids]
        return jnp.einsum('bsi,boi->bso', x, w)
    x = x + _L0_cond_ref(x, itok_B_0_15, L0_cond_weights)
    x = x + _L1_cond_ref(x, L1_cond_weight, itok_B_3_7)
    return x

_drawn_inputs = setup_inputs


def setup_inputs(seed=0):
    import zlib

    import numpy as np

    out = dict(_drawn_inputs(seed))
    spreads = {}
    factors = {}
    for name, (base, spread) in spreads.items():
        noise = np.random.default_rng([zlib.crc32(name.encode()), seed]).standard_normal(out[name].shape)
        drawn = base * np.exp(spread * noise) if base else spread * noise
        out[name] = jnp.asarray(drawn.astype(out[name].dtype))
    for name, factor in factors.items():
        out[name] = (out[name] * factor).astype(out[name].dtype)
    return out
```

```python
from contextlib import ExitStack

import concourse.bass as bass
from concourse import mybir

F32 = mybir.dt.float32
F32R = mybir.dt.float32r
I32 = mybir.dt.int32
ALU = mybir.AluOpType
COPY = mybir.ActivationFunctionType.Copy
AX_X = mybir.AxisListType.X
ds = bass.ds

P = 128
B = 32
T = 2048
NC = 512
CHUNKS = T // NC
STEPS = CHUNKS * B
KB = T // P
SQ = 32
QUAD = P // SQ
PIECES = 4
KP = KB // PIECES
PF = SQ * KP
OA = NC // SQ
WBUF = KB * NC
MAXQ = 32
DMA = 16


def build(nc, x, cond, adapter, w0, w1, out):
    ctx = ExitStack()
    with ctx:
        def sb(name, shape, dt=F32):
            return ctx.enter_context(nc.sbuf_tensor(name, shape, dt))

        def ps(name, shape):
            return ctx.enter_context(nc.psum_tensor(name, shape, F32))

        def sem(name):
            return ctx.enter_context(nc.semaphore(name))

        y_dram = nc.dram_tensor("y_scratch", (B, P, T), F32, kind="Internal").ap()

        w_high = sb("w_high", [P, 2 * WBUF], F32R)
        w_low = sb("w_low", [P, 2 * WBUF], F32R)
        w_nat = [sb(f"w_nat{s}", [P, OA * PF]) for s in range(2)]
        w_turn = sb("w_turn", [P, KP * NC])
        y_high = [sb(f"y_high{s}", [P, KB * P], F32R) for s in range(2)]
        y_low = [sb(f"y_low{s}", [P, KB * P], F32R) for s in range(2)]
        seq = [sb(f"seq{s}", [P, T]) for s in range(2)]
        y_raw = sb("y_raw", [P, KB * P])
        a0 = [sb(f"a0_{s}", [P, P]) for s in range(2)]
        out_sb = [sb(f"out_sb{s}", [P, NC]) for s in range(2)]
        ident_zero = sb("ident_zero", [P, (2 * CHUNKS - 1) * P])
        ident = ident_zero[:, (CHUNKS - 1) * P:CHUNKS * P]

        chunk_seq, counting, key_row, not_before, at_step, own, before, before_group, hot = (
            y_raw[:, i * P:(i + 1) * P] for i in range(9))
        at_group, past_group = hot[:, 0:MAXQ], hot[:, MAXQ:2 * MAXQ]
        part_i = sb("part_i", [P, 1], I32)
        seq_i = sb("seq_i", [P, 1], I32)
        quad_i = sb("quad_i", [P, 1], I32)
        ids_row = sb("ids_row", [P, B], I32)
        cond_i = sb("cond_i", [B, 1], I32)
        cols = sb("cols", [P, 16])
        COL = {n: i for i, n in enumerate(
            ["seq", "quad", "cond", "column", "key", "group_key", "rank", "start", "first", "row", "first_row",
             "first_quad", "group", "group2", "one"])}
        def col(name):
            return cols[:, COL[name]:COL[name] + 1]
        step_tab = sb("step_tab", [1, 3 * STEPS], I32)
        group_of = sb("group_of", [1, STEPS], I32)
        buffer_of = sb("buffer_of", [1, STEPS], I32)
        group_tab = sb("group_tab", [1, 3 * MAXQ + 1], I32)

        y_ps = ps("y_ps", [P, KB * P])
        out_ps = [ps(f"out_ps{s}", [P, NC]) for s in range(2)]
        sort_ps = out_ps[1]
        GROUP_PS, STEP_PS, OF_PS, TAB_PS = 0, 4, 4, 4

        ids_loaded = sem("ids_loaded")
        consts_made = sem("consts_made")
        sort_step = sem("sort_step")
        sort_mm = sem("sort_mm")
        group_tables = sem("group_tables")
        step_tables = sem("step_tables")
        w_loaded = [sem(f"w_loaded{s}") for s in range(2)]
        w_diag = sem("w_diag")
        w_turned = sem("w_turned")
        w_rounded = sem("w_rounded")
        w_ready = sem("w_ready")
        seq_loaded = [sem(f"seq_loaded{s}") for s in range(2)]
        a_loaded = [sem(f"a_loaded{s}") for s in range(2)]
        a_ready = sem("a_ready")
        y_made = sem("y_made")
        y_high_made = sem("y_high_made")
        y_raw_made = sem("y_raw_made")
        y_split = sem("y_split")
        y_stored = sem("y_stored")
        gemm_done = sem("gemm_done")
        out_free = sem("out_free")
        out_stored = [sem(f"out_stored{s}") for s in range(2)]

        block = ctx.enter_context(nc.Block())

        def table(eng, tab, i, most, at=0):
            return eng.value_load(tab[0:1, ds(i + at, 1)], min_val=0, max_val=most)

        @block.sync
        def _(sp):
            sp.dma_start(ids_row[:], adapter.partition_broadcast(P)).then_inc(ids_loaded, DMA)
            sp.dma_start(cond_i[:], cond.rearrange("(b o) -> b o", o=1)).then_inc(ids_loaded, DMA)
            sp.wait_ge(step_tables, 1)
            groups = sp.value_load(group_of[0:1, STEPS - 1:STEPS], min_val=3, max_val=MAXQ - 1) + 1
            rows = w1.rearrange("e o i -> (e o) i")
            with sp.Fori(0, groups) as q:
                row = table(sp, group_tab, q, rows.shape[0] - NC)
                chunk = rows[ds(row, NC), :].rearrange("(a p) i -> p a i", p=SQ)
                for m in range(PIECES):
                    s = m % 2
                    sp.wait_ge(w_turned, q * PIECES + m + 1)
                    for b in range(QUAD):
                        i0 = (m * QUAD + b) * PF
                        sp.dma_start(w_nat[s][b * SQ:(b + 1) * SQ, :].rearrange("p (a f) -> p a f", f=PF),
                                     chunk[:, :, i0:i0 + PF]).then_inc(w_loaded[s], DMA)

        @block.gpsimd
        def _(pool):
            nc.gpsimd.memset(ident_zero[:], 0.0).then_inc(consts_made, 1)
            nc.gpsimd.iota(chunk_seq.rearrange("p (c b) -> p c b", b=B), [[256, CHUNKS], [1, B]], channel_multiplier=0,
                           allow_small_or_imprecise_dtypes=True).then_inc(consts_made, 1)
            nc.gpsimd.iota(counting, [[1, P]], channel_multiplier=0,
                           allow_small_or_imprecise_dtypes=True).then_inc(consts_made, 1)
            nc.gpsimd.iota(part_i[:], [[0, 1]], channel_multiplier=1).then_inc(consts_made, 1)
            pool.wait_ge(consts_made, 1)
            nc.gpsimd.affine_select(out=ident, in_=ident, compare_op=ALU.not_equal, fill=1.0, base=0,
                                    pattern=[[-1, P]], channel_multiplier=1).then_inc(consts_made, 1)
            pool.wait_ge(consts_made, 5)

            def first_weights(t, s):
                pool.wait_ge(a_loaded[s], (t - s) * (DMA // 2) + DMA)
                nc.gpsimd.tensor_tensor(a0[s][:], a0[s][:], ident, ALU.add).then_inc(a_ready, 1)

            def low_part(t, s, raw):
                pool.wait_ge(y_high_made, t + 1)
                nc.gpsimd.tensor_tensor(y_low[s][:], raw, y_high[s][:], ALU.subtract).then_inc(y_split, 1)

            def from_y_raw(t, s):
                pool.wait_ge(y_raw_made, t + 1)
                low_part(t, s, y_raw[:])

            first_weights(0, 0)
            with pool.Fori(0, B - 2, 2) as t:
                for s in range(2):
                    first_weights(t + s + 1, 1 - s)
                    from_y_raw(t + s, s)
            first_weights(B - 1, 1)
            from_y_raw(B - 2, 0)
            from_y_raw(B - 1, 1)
            with pool.Fori(B, STEPS - 1, 2) as t:
                for s in range(2):
                    low_part(t + s, s, seq[s][:])

        @block.scalar
        def _(act):
            act.sem_inc(out_free, 2)

            def load_x(t, s):
                b = table(act, step_tab, t, B - 1)
                c = table(act, step_tab, t, w0.shape[0] - 1, STEPS)
                act.dma_start(seq[s][:], x[ds(b, 1), :, :].rearrange("o c t -> (o c) t")).then_inc(seq_loaded[s], DMA)
                act.dma_start(a0[s][:], w0[ds(c, 1), :, :].rearrange("o c d -> (o c) d")).then_inc(a_loaded[s], DMA)

            def load_y(t, s):
                b = table(act, step_tab, t, B - 1)
                act.dma_start(seq[s][:], y_dram[ds(b, 1), :, :].rearrange("o p n -> (o p) n")).then_inc(seq_loaded[s], DMA)

            def high_part(t, s, raw, first=False):
                if not first:
                    act.wait_ge(gemm_done, t)
                nc.scalar.activation(y_high[s][:], raw, COPY).then_inc(y_high_made, 1)

            def take_y(t, s, first=False):
                act.wait_ge(y_made, t + 1)
                high_part(t, s, y_ps[:], first)
                if not first:
                    act.wait_ge(y_stored, t * DMA)
                    act.wait_ge(y_split, t)
                nc.scalar.activation(y_raw[:], y_ps[:], COPY).then_inc(y_raw_made, 1)
                b = table(act, step_tab, t, B - 1)
                act.wait_ge(y_raw_made, t + 1)
                act.dma_start(y_dram[ds(b, 1), :, :].rearrange("o p n -> (o p) n"), y_raw[:]).then_inc(y_stored, DMA)

            def take_result(t, s, first=False):
                b = table(act, step_tab, t, B - 1)
                n0 = table(act, step_tab, t, T - NC, 2 * STEPS)
                if not first:
                    act.wait_ge(out_stored[s], (t - s) * (DMA // 2))
                act.wait_ge(gemm_done, t + 2)
                nc.scalar.activation(out_sb[s][:], out_ps[s][:], COPY).then_inc(out_free, 1)
                act.wait_ge(out_free, t + 3)
                act.dma_start(out[ds(b, 1), :, ds(n0, NC)].rearrange("o d n -> (o d) n"), out_sb[s][:])\
                   .then_inc(out_stored[s], DMA)

            def step_0(t, s, first=False):
                act.wait_ge(y_made, t + 2)
                load_x(t + 3, 1 - s)
                take_y(t + 1, 1 - s)
                take_result(t, s, first)

            def step_n(t, s, load=True):
                act.wait_ge(seq_loaded[1 - s], (t + s) * (DMA // 2) + DMA)
                high_part(t + 1, 1 - s, seq[1 - s][:])
                if load:
                    act.wait_ge(y_split, t + 2)
                    load_y(t + 3, 1 - s)
                take_result(t, s)

            act.wait_ge(step_tables, 1)
            load_x(0, 0)
            load_x(1, 1)
            act.wait_ge(y_made, 1)
            load_x(2, 0)
            take_y(0, 0, first=True)
            step_0(0, 0, first=True)
            step_0(1, 1, first=True)
            with act.Fori(2, B - 4, 2) as t:
                step_0(t, 0)
                step_0(t + 1, 1)
            step_0(B - 4, 0)
            for t in (B - 3, B - 2):
                act.wait_ge(y_made, t + 2)
                load_y(t + 3, 1 - t % 2)
                take_y(t + 1, 1 - t % 2)
                take_result(t, t % 2)
            act.wait_ge(y_stored, B * DMA)
            with act.Fori(B - 1, STEPS - 4, 2) as t:
                act_t = t
                act.wait_ge(seq_loaded[0], (act_t + 1) * (DMA // 2) + DMA)
                high_part(act_t + 1, 0, seq[0][:])
                act.wait_ge(y_split, act_t + 2)
                load_y(act_t + 3, 0)
                take_result(act_t, 1)
                act_t = t + 1
                act.wait_ge(seq_loaded[1], (act_t) * (DMA // 2) + DMA)
                high_part(act_t + 1, 1, seq[1][:])
                act.wait_ge(y_split, act_t + 2)
                load_y(act_t + 3, 1)
                take_result(act_t, 0)
            for t in (STEPS - 3, STEPS - 2):
                act.wait_ge(seq_loaded[1 - t % 2], (t + 1) // 2 * DMA + DMA)
                high_part(t + 1, 1 - t % 2, seq[1 - t % 2][:])
                take_result(t, t % 2)
            take_result(STEPS - 1, 1)
            for s in range(2):
                act.wait_ge(out_stored[s], STEPS // 2 * DMA)

        @block.vector
        def _(dve):
            done = [0]

            def link(instruction):
                done[0] += 1
                instruction.then_inc(sort_step, 1)
                dve.wait_ge(sort_step, done[0])

            dve.sem_inc(w_turned, 2)
            nc.vector.memset(cols[:], 0.0).then_inc(sort_step, 1)
            done[0] = 1
            dve.wait_ge(consts_made, 5)
            nc.vector.tensor_scalar(seq_i[:], part_i[:], B - 1, None, ALU.bitwise_and).then_inc(sort_step, 1)
            nc.vector.tensor_scalar(quad_i[:], part_i[:], P - B, None, ALU.bitwise_and).then_inc(sort_step, 1)
            done[0] += 2
            dve.wait_ge(sort_step, done[0])
            nc.vector.tensor_copy(col("seq"), seq_i[:]).then_inc(sort_step, 1)
            nc.vector.tensor_copy(col("quad"), quad_i[:]).then_inc(sort_step, 1)
            nc.vector.tensor_scalar(col("column"), quad_i[:], NC // B, None, ALU.mult).then_inc(sort_step, 1)
            nc.vector.memset(col("one"), 1.0).then_inc(sort_step, 1)
            done[0] += 4
            dve.wait_ge(ids_loaded, 2 * DMA)
            link(nc.vector.scalar_tensor_tensor(
                out=key_row.rearrange("p (c b) -> p c b", b=B),
                in0=ids_row[:].unsqueeze(1).to_broadcast([P, CHUNKS, B]), scalar=float(B),
                in1=chunk_seq.rearrange("p (c b) -> p c b", b=B), op0=ALU.mult, op1=ALU.add))
            nc.vector.tensor_copy(col("cond")[0:B, :], cond_i[:]).then_inc(sort_step, 1)
            done[0] += 1
            link(nc.vector.tensor_tensor(own, key_row, ident, ALU.mult))
            link(nc.vector.reduce_sum(col("key"), own, AX_X))
            link(nc.vector.tensor_tensor(col("group_key"), col("key"), col("seq"), ALU.subtract))
            nc.vector.tensor_scalar(before, key_row, col("key"), None, ALU.is_lt).then_inc(sort_step, 1)
            nc.vector.tensor_scalar(before_group, key_row, col("group_key"), None, ALU.is_lt).then_inc(sort_step, 1)
            done[0] += 2
            link(nc.vector.tensor_scalar(not_before, key_row, col("key"), None, ALU.is_ge))
            nc.vector.reduce_sum(col("rank"), before, AX_X).then_inc(sort_step, 1)
            done[0] += 1
            link(nc.vector.reduce_sum(col("start"), before_group, AX_X))
            nc.vector.tensor_tensor(col("first"), col("rank"), col("start"), ALU.is_equal).then_inc(sort_step, 1)
            done[0] += 1
            link(nc.vector.tensor_scalar(at_step, counting, col("rank"), None, ALU.is_equal))
            assert done[0] == SORTED
            link(nc.vector.tensor_scalar(col("row"), col("quad"), float(NC // B - T // B * 256 // B), None, ALU.mult))
            link(nc.vector.scalar_tensor_tensor(out=col("row"), in0=col("group_key"), scalar=float(T // B),
                                                in1=col("row"), op0=ALU.mult, op1=ALU.add))
            nc.vector.tensor_tensor(col("first_row"), col("row"), col("first"), ALU.mult).then_inc(sort_step, 1)
            nc.vector.tensor_tensor(col("first_quad"), col("quad"), col("first"), ALU.mult).then_inc(sort_step, 1)
            done[0] += 2
            dve.wait_ge(sort_mm, 1)
            nc.vector.tensor_scalar(col("group"), sort_ps[:, 0:1], -1.0, None, ALU.add).then_inc(sort_step, 1)
            done[0] += 1
            link(nc.vector.tensor_scalar(col("group2"), sort_ps[:, 0:1], 1.0, None, ALU.add))
            nc.vector.tensor_scalar(at_group, counting[:, 0:MAXQ], col("group"), None, ALU.is_equal).then_inc(sort_step, 1)
            nc.vector.tensor_scalar(past_group, counting[:, 0:MAXQ], col("group2"), None, ALU.is_ge).then_inc(sort_step, 1)
            done[0] += 2
            assert done[0] == GROUPED
            dve.wait_ge(sort_mm, 2)
            o = 4
            link(nc.vector.tensor_copy(group_of[:], sort_ps[0:1, o:o + STEPS]))
            o += STEPS
            nc.vector.tensor_copy(group_tab[:, 0:MAXQ], sort_ps[0:1, o:o + MAXQ]).then_inc(sort_step, 1)
            nc.vector.tensor_scalar(group_tab[:, MAXQ:2 * MAXQ], sort_ps[0:1, o + MAXQ:o + 2 * MAXQ], -float(P // SQ),
                                    float((CHUNKS - 1) * P), ALU.mult, ALU.add).then_inc(sort_step, 1)
            nc.vector.tensor_scalar(group_tab[:, 2 * MAXQ:3 * MAXQ], sort_ps[0:1, o + 2 * MAXQ:o + 3 * MAXQ], 1.0, None,
                                    ALU.add).then_inc(sort_step, 1)
            nc.vector.tensor_scalar(buffer_of[:], group_of[:], 1, WBUF.bit_length() - 1, ALU.bitwise_and,
                                    ALU.logical_shift_left).then_inc(sort_step, 1)
            nc.vector.tensor_copy(step_tab[:], y_ps[0:1, 0:3 * STEPS]).then_inc(sort_step, 1)
            done[0] += 5
            dve.wait_ge(sort_step, done[0])
            dve.sem_inc(step_tables, 1)

            groups = dve.value_load(group_of[0:1, STEPS - 1:STEPS], min_val=3, max_val=MAXQ - 1) + 1
            with dve.Fori(0, groups, 2) as q2:
                eyes = [table(dve, group_tab, q2 + buf, (CHUNKS - 1) * P, MAXQ) for buf in range(2)]
                frees = [dve.value_load(group_tab[0:1, ds(q2 + buf + 2 * MAXQ, 1)], min_val=1, max_val=STEPS + 1)
                         for buf in range(2)]
                for buf in range(2):
                    q, eye = q2 + buf, eyes[buf]
                    dve.wait_ge(gemm_done, frees[buf])
                    for m in range(PIECES):
                        s = m % 2
                        n = q * PIECES + m
                        nat = w_nat[s][:].rearrange("p (a c r) -> p r a c", r=KP, c=SQ)
                        turned = w_turn[:].rearrange("p (r a c) -> p r a c", r=KP, c=SQ)
                        at = buf * WBUF + m * KP * NC
                        high = w_high[:, at:at + KP * NC]
                        low = w_low[:, at:at + KP * NC]
                        dve.wait_ge(w_loaded[s], (q * 2 + m // 2 + 1) * (QUAD * DMA))
                        squares = bass.AP(w_nat[s], 0, [[OA * PF, P], [KP * PF, QUAD], [PF + SQ, KP], [1, SQ]])
                        one = ident_zero[:, ds(eye + m * P, P)]
                        one = one.rearrange("p (b c) -> p b c", c=SQ).unsqueeze(2).to_broadcast([P, QUAD, KP, SQ])
                        nc.vector.tensor_tensor(squares, squares, one, ALU.add).then_inc(w_diag, 1)
                        dve.wait_ge(w_diag, n + 1)
                        nc.vector.transpose(turned, nat).then_inc(w_turned, 1)
                        dve.wait_ge(w_turned, n + 3)
                        nc.vector.tensor_copy(high, w_turn[:]).then_inc(w_rounded, 1)
                        dve.wait_ge(w_rounded, n + 1)
                        nc.vector.tensor_tensor(low, w_turn[:], high, ALU.subtract).then_inc(w_ready, 1)
                        dve.wait_ge(w_ready, n + 1)

        @block.tensor
        def _(pe):
            pe.sem_inc(gemm_done, 1)
            pe.wait_ge(sort_step, SORTED)
            nc.tensor.matmul(sort_ps[:, 0:1], not_before, col("first"), start=True, stop=True).then_inc(sort_mm, 1)
            for i, name in enumerate(["seq", "cond", "column"]):
                nc.tensor.matmul(y_ps[0:1, i * STEPS:(i + 1) * STEPS], col(name), at_step, start=True, stop=True)
            pe.wait_ge(sort_step, GROUPED)
            o = 4
            nc.tensor.matmul(sort_ps[0:1, o:o + STEPS], col("group"), at_step, start=True, stop=True)
            o += STEPS
            for name, taken in (("first_row", at_group), ("first_quad", at_group), ("one", past_group)):
                last = nc.tensor.matmul(sort_ps[0:1, o:o + MAXQ], col(name), taken, start=True, stop=True)
                o += MAXQ
            last.then_inc(sort_mm, 1)
            pe.wait_ge(step_tables, 1)

            def first_layer(t, s, first=False):
                pe.wait_ge(seq_loaded[s], (t - s) * (DMA // 2) + DMA)
                pe.wait_ge(a_ready, t + 1)
                if not first:
                    pe.wait_ge(y_raw_made, t)
                blocks = seq[s][:].rearrange("c (m j r) -> c m r j", m=PIECES, r=KP)
                for k in range(KB):
                    last = nc.tensor.matmul(y_ps[:, k * P:(k + 1) * P], blocks[:, k // KP, k % KP, :], a0[s][:],
                                            start=True, stop=True)
                last.then_inc(y_made, 1)

            def gemm(t, s):
                q = table(pe, group_of, t, MAXQ - 1)
                at = table(pe, buffer_of, t, WBUF)
                pe.wait_ge(y_high_made, t + 1)
                pe.wait_ge(out_free, t + 1)
                for k in range(KB):
                    if k % KP == 0:
                        pe.wait_ge(w_ready, q * PIECES + (k // KP + 1))
                    ys = y_high[s][:, k * P:(k + 1) * P]
                    nc.tensor.matmul(out_ps[s][:], ys, w_high[:, ds(at + k * NC, NC)], start=(k == 0), stop=False)
                    nc.tensor.matmul(out_ps[s][:], ys, w_low[:, ds(at + k * NC, NC)], start=False, stop=False)
                pe.wait_ge(y_split, t + 1)
                for k in range(KB):
                    ys = y_low[s][:, k * P:(k + 1) * P]
                    last = nc.tensor.matmul(out_ps[s][:], ys, w_high[:, ds(at + k * NC, NC)],
                                            start=False, stop=(k == KB - 1))
                last.then_inc(gemm_done, 1)

            first_layer(0, 0, first=True)
            with pe.Fori(0, B - 2, 2) as t:
                for s in range(2):
                    first_layer(t + s + 1, 1 - s)
                    gemm(t + s, s)
            first_layer(B - 1, 1)
            gemm(B - 2, 0)
            gemm(B - 1, 1)
            with pe.Fori(B, STEPS - 1, 2) as t:
                for s in range(2):
                    gemm(t + s, s)


SORTED = 19
GROUPED = 27


_INS = ["x", "itok_B_0_15", "itok_B_3_7", "L0_cond_weights", "L1_cond_weight"]


def kernel(**inputs):
    import numpy as np
    import concourse.bacc as bacc
    from concourse.bass_utils import run_bass_kernel_spmd

    nc = bacc.Bacc("TRN2", target_bir_lowering=False, num_devices=1, dynamic_dma_scratch_size=1024)
    arrays, args = {}, []
    for name in _INS:
        a = np.ascontiguousarray(inputs[name])
        arrays[f"in_{name}"] = a
        args.append(nc.dram_tensor(f"in_{name}", a.shape, mybir.dt.from_np(a.dtype), kind="ExternalInput").ap())
    args.append(nc.dram_tensor("out", (B, P, T), F32, kind="ExternalOutput").ap())
    build(nc, *args)
    r = run_bass_kernel_spmd(nc, [arrays], core_ids=[0])
    return r.results[0]["out"]
```

```python
from contextlib import ExitStack

import concourse.bass as bass
from concourse import mybir

F32 = mybir.dt.float32
F32R = mybir.dt.float32r
I32 = mybir.dt.int32
ALU = mybir.AluOpType
COPY = mybir.ActivationFunctionType.Copy
AX_X = mybir.AxisListType.X
ds = bass.ds

P = 128
B = 32
T = 2048
NC = 512
CHUNKS = T // NC
STEPS = CHUNKS * B
KB = T // P
SQ = 32
QUAD = P // SQ
PIECES = 4
KP = KB // PIECES
PF = SQ * KP
XF = T // QUAD
OA = NC // SQ
WBUF = KB * NC
HALF = KP * NC // 2
MAXQ = 32
DMA = 16


def build(nc, x, cond, adapter, w0, w1, out):
    ctx = ExitStack()
    with ctx:
        def sb(name, shape, dt=F32):
            return ctx.enter_context(nc.sbuf_tensor(name, shape, dt))

        def ps(name, shape):
            return ctx.enter_context(nc.psum_tensor(name, shape, F32))

        def sem(name):
            return ctx.enter_context(nc.semaphore(name))

        w_high = sb("w_high", [P, 2 * WBUF], F32R)
        w_low = sb("w_low", [P, 2 * WBUF], F32R)
        w_nat = [sb(f"w_nat{s}", [P, OA * PF]) for s in range(2)]
        w_turn = sb("w_turn", [P, KP * NC])
        x_nat = sb("x_nat", [P, QUAD * XF])
        x_turn = sb("x_turn", [P, KB * P])
        x_high = [sb(f"x_high{s}", [P, KB * P], F32R) for s in range(2)]
        x_low = [sb(f"x_low{s}", [P, KB * P], F32R) for s in range(2)]
        z_raw = sb("z_raw", [P, NC])
        z_high = sb("z_high", [P, NC], F32R)
        z_low = sb("z_low", [P, NC], F32R)
        a_full = sb("a_full", [P, P])
        a_high = sb("a_high", [P, P], F32R)
        a_low = sb("a_low", [P, P], F32R)
        out_sb = [sb(f"out_sb{s}", [P, NC]) for s in range(2)]
        ident = sb("ident", [P, P])

        chunk_seq, counting, key_row, not_before, at_step, own, before, before_group, hot = (
            x_turn[:, i * P:(i + 1) * P] for i in range(9))
        by_group = hot[:, 0:2 * MAXQ]
        part_i = sb("part_i", [P, 1], I32)
        seq_i = sb("seq_i", [P, 1], I32)
        quad_i = sb("quad_i", [P, 1], I32)
        ids_row = sb("ids_row", [P, B], I32)
        cond_i = sb("cond_i", [P, 1], I32)
        cols = sb("cols", [P, 15])
        COLS = ["seq", "cond", "result", "group", "first_row", "first_eye", "one",
                "quad", "key", "group_key", "rank", "start", "first", "row", "next_group"]

        def col(first, last=None):
            return cols[:, COLS.index(first):COLS.index(last or first) + 1]
        SEQ, COND, RESULT, GROUP = range(4)
        step_tab = sb("step_tab", [4, STEPS + 2], I32)
        buffer_tab = sb("buffer_tab", [4, STEPS + 2], I32)
        ROW, EYE, FIRST = range(3)
        group_tab = sb("group_tab", [3, 2 * MAXQ + 2], I32)

        z_ps = [ps(f"z_ps{s}", [P, NC]) for s in range(2)]
        out_ps = ps("out_ps", [P, NC])
        group_ps, group_tab_ps, step_ps = z_ps[1][:, 0:1], z_ps[1][0:3, P:P + 2 * MAXQ], z_ps[0][0:4, 0:STEPS]

        ids_loaded = sem("ids_loaded")
        consts_made = sem("consts_made")
        sort_step = sem("sort_step")
        sort_mm = sem("sort_mm")
        group_tables = sem("group_tables")
        step_tables = sem("step_tables")
        w_loaded = [sem(f"w_loaded{s}") for s in range(2)]
        w_diag = sem("w_diag")
        w_half_turned = sem("w_half_turned")
        w_turned = sem("w_turned")
        w_rounded = sem("w_rounded")
        w_ready = sem("w_ready")
        x_loaded = sem("x_loaded")
        x_turned = sem("x_turned")
        x_high_made = sem("x_high_made")
        x_split = sem("x_split")
        a_loaded = sem("a_loaded")
        a_ready = sem("a_ready")
        a_high_made = sem("a_high_made")
        a_split = sem("a_split")
        gemm_done = sem("gemm_done")
        z_copied = sem("z_copied")
        z_split = sem("z_split")
        out_made = sem("out_made")
        out_copied = sem("out_copied")
        out_stored = [sem(f"out_stored{s}") for s in range(2)]

        block = ctx.enter_context(nc.Block())

        def by_step(eng, row, t, most, tab=step_tab):
            return eng.value_load(tab[row:row + 1, ds(t, 1)], min_val=0, max_val=most)

        def of_group(eng, row, q, most):
            return eng.value_load(group_tab[row:row + 1, ds(q, 1)], min_val=0, max_val=most)

        def count_groups(eng):
            return by_step(eng, GROUP, STEPS - 1, MAXQ - 1) + 1

        @block.sync
        def _(sp):
            sp.dma_start(ids_row[:], adapter.partition_broadcast(P)).then_inc(ids_loaded, DMA)
            sp.dma_start(cond_i[:], bass.AP(cond.tensor, 0, [[0, CHUNKS], [1, B], [1, 1]])).then_inc(ids_loaded, DMA)
            sp.wait_ge(group_tables, 1)
            rows = w1.rearrange("e o i -> (e o) i")

            def load_group(q):
                row = of_group(sp, ROW, q, rows.shape[0] - NC)
                chunk = rows[ds(row, NC), :].rearrange("(a p) i -> p a i", p=SQ)
                for m in range(PIECES):
                    s = m % 2
                    sp.wait_ge(w_turned, q * PIECES + m + 1)
                    for b in range(QUAD):
                        i0 = b * (T // QUAD) + m * PF
                        sp.dma_start(w_nat[s][b * SQ:(b + 1) * SQ, :].rearrange("p (a f) -> p a f", f=PF),
                                     chunk[:, :, i0:i0 + PF]).then_inc(w_loaded[s], DMA)

            load_group(0)
            sp.wait_ge(step_tables, 1)
            with sp.Fori(1, count_groups(sp)) as q:
                load_group(q)

        @block.gpsimd
        def _(pool):
            nc.gpsimd.memset(ident[:], 0.0).then_inc(consts_made, 1)
            nc.gpsimd.iota(chunk_seq.rearrange("p (c b) -> p c b", b=B), [[256, CHUNKS], [1, B]], channel_multiplier=0,
                           allow_small_or_imprecise_dtypes=True).then_inc(consts_made, 1)
            nc.gpsimd.iota(counting, [[1, P]], channel_multiplier=0,
                           allow_small_or_imprecise_dtypes=True).then_inc(consts_made, 1)
            nc.gpsimd.iota(part_i[:], [[0, 1]], channel_multiplier=1).then_inc(consts_made, 1)
            pool.wait_ge(consts_made, 1)
            nc.gpsimd.affine_select(out=ident[:], in_=ident[:], compare_op=ALU.not_equal, fill=1.0, base=0,
                                    pattern=[[-1, P]], channel_multiplier=1).then_inc(consts_made, 1)
            pool.wait_ge(consts_made, 5)

            def x_rest(t, s):
                pool.wait_ge(x_high_made, t + 1)
                nc.gpsimd.tensor_tensor(x_low[s][:], x_turn[:], x_high[s][:], ALU.subtract).then_inc(x_split, 1)

            def z_rest(t):
                pool.wait_ge(z_copied, 2 * t + 2)
                nc.gpsimd.tensor_tensor(z_low[:], z_raw[:], z_high[:], ALU.subtract).then_inc(z_split, 1)

            def a_parts(t):
                pool.wait_ge(a_loaded, (t + 1) * DMA)
                nc.gpsimd.tensor_tensor(a_full[:], a_full[:], ident[:], ALU.add).then_inc(a_ready, 1)
                pool.wait_ge(a_high_made, t + 1)
                nc.gpsimd.tensor_tensor(a_low[:], a_full[:], a_high[:], ALU.subtract).then_inc(a_split, 1)

            x_rest(0, 0)
            x_rest(1, 1)
            a_parts(0)
            with pool.Fori(0, STEPS // 2 - 1) as p:
                for s in (1, 0):
                    t = 2 * p + (2 - s)
                    z_rest(t - 1)
                    x_rest(t + 1, 1 - s)
                    a_parts(t)
            z_rest(STEPS - 2)
            a_parts(STEPS - 1)
            z_rest(STEPS - 1)

        @block.scalar
        def _(act):
            act.sem_inc(out_copied, 1)

            def load_x(t):
                b = by_step(act, SEQ, t, B - 1)
                for j in range(QUAD):
                    act.dma_start(x_nat[j * SQ:(j + 1) * SQ, :].rearrange("p (a f) -> p a f", a=QUAD),
                                  x[ds(b, 1), :, j * XF:(j + 1) * XF].rearrange("o (a p) f -> p (o a) f", p=SQ))\
                        .then_inc(x_loaded, DMA)

            def load_a(t):
                c = by_step(act, COND, t, w0.shape[0] - 1)
                act.dma_start(a_full[:], w0[ds(c, 1), :, :].rearrange("o c d -> (o c) d")).then_inc(a_loaded, DMA)

            def take_x(t, s):
                act.wait_ge(x_turned, t + 1)
                nc.scalar.activation(x_high[s][:], x_turn[:], COPY).then_inc(x_high_made, 1)

            def take_z(t, s):
                act.wait_ge(gemm_done, t + 2)
                nc.scalar.activation(z_raw[:], z_ps[s][:], COPY).then_inc(z_copied, 1)
                nc.scalar.activation(z_high[:], z_ps[s][:], COPY).then_inc(z_copied, 1)

            def take_out(t, s, stored):
                at = by_step(act, RESULT, t, B * P * T - NC)
                if stored is not None:
                    act.wait_ge(out_stored[s], stored * DMA)
                act.wait_ge(out_made, t + 1)
                nc.scalar.activation(out_sb[s][:], out_ps[:], COPY).then_inc(out_copied, 1)
                act.wait_ge(out_copied, t + 2)
                act.dma_start(bass.AP(out.tensor, at, [[T, P], [1, NC]]), out_sb[s][:]).then_inc(out_stored[s], DMA)

            def take_a(t):
                act.wait_ge(a_ready, t + 1)
                nc.scalar.activation(a_high[:], a_full[:], COPY).then_inc(a_high_made, 1)

            def beside(t, s, stored, more=True):
                take_z(t - 1, 1 - s)
                if more:
                    take_x(t + 1, 1 - s)
                    load_x(t + 2)
                act.wait_ge(a_split, t)
                load_a(t)
                take_out(t - 1, 1 - s, stored)
                take_a(t)

            act.wait_ge(consts_made, 5)
            nc.scalar.activation(out_sb[0][:, 0:1], ident[:, 0:1], COPY)

            act.wait_ge(step_tables, 1)
            load_x(0)
            load_a(0)
            take_x(0, 0)
            load_x(1)
            for m in range(PIECES):
                for h in range(2):
                    if h == 0:
                        act.wait_ge(w_half_turned, m + 1)
                    else:
                        act.wait_ge(w_turned, m + 3)
                    at = m * KP * NC + h * HALF
                    nc.scalar.activation(w_high[:, at:at + HALF], w_turn[:, h * HALF:(h + 1) * HALF], COPY)\
                        .then_inc(w_rounded, 1)
            take_x(1, 1)
            load_x(2)
            take_a(0)

            beside(1, 1, None)
            beside(2, 0, None)
            with act.Fori(1, STEPS // 2 - 1) as p:
                beside(2 * p + 1, 1, p)
                beside(2 * p + 2, 0, p)
            beside(STEPS - 1, 1, STEPS // 2 - 1, more=False)
            take_z(STEPS - 1, 1)
            take_out(STEPS - 1, 1, STEPS // 2 - 1)
            for s in range(2):
                act.wait_ge(out_stored[s], STEPS // 2 * DMA)

        @block.vector
        def _(dve):
            done = [0]

            def link(instruction):
                done[0] += 1
                instruction.then_inc(sort_step, 1)
                dve.wait_ge(sort_step, done[0])

            dve.sem_inc(w_turned, 2)
            nc.vector.memset(cols[:], 0.0).then_inc(sort_step, 1)
            nc.vector.memset(step_tab[:], 0).then_inc(sort_step, 1)
            done[0] = 2
            dve.wait_ge(consts_made, 5)
            nc.vector.tensor_scalar(seq_i[:], part_i[:], B - 1, None, ALU.bitwise_and).then_inc(sort_step, 1)
            nc.vector.tensor_scalar(quad_i[:], part_i[:], P - B, None, ALU.bitwise_and).then_inc(sort_step, 1)
            done[0] += 2
            dve.wait_ge(sort_step, done[0])
            nc.vector.tensor_copy(col("seq"), seq_i[:]).then_inc(sort_step, 1)
            nc.vector.tensor_copy(col("quad"), quad_i[:]).then_inc(sort_step, 1)
            nc.vector.tensor_scalar(col("result"), quad_i[:], float(NC // B), None, ALU.mult).then_inc(sort_step, 1)
            nc.vector.memset(col("one"), 1.0).then_inc(sort_step, 1)
            done[0] += 4
            dve.wait_ge(sort_step, done[0])
            link(nc.vector.scalar_tensor_tensor(out=col("result"), in0=col("seq"), scalar=float(P * T),
                                                in1=col("result"), op0=ALU.mult, op1=ALU.add))
            dve.wait_ge(ids_loaded, 2 * DMA)
            link(nc.vector.scalar_tensor_tensor(
                out=key_row.rearrange("p (c b) -> p c b", b=B),
                in0=ids_row[:].unsqueeze(1).to_broadcast([P, CHUNKS, B]), scalar=float(B),
                in1=chunk_seq.rearrange("p (c b) -> p c b", b=B), op0=ALU.mult, op1=ALU.add))
            link(nc.vector.tensor_tensor(own, key_row, ident[:], ALU.mult))
            link(nc.vector.reduce_sum(col("key"), own, AX_X))
            nc.vector.tensor_scalar(before, key_row, col("key"), None, ALU.is_lt).then_inc(sort_step, 1)
            nc.vector.tensor_tensor(col("group_key"), col("key"), col("seq"), ALU.subtract).then_inc(sort_step, 1)
            nc.vector.tensor_scalar(not_before, key_row, col("key"), None, ALU.is_ge).then_inc(sort_step, 1)
            done[0] += 3
            dve.wait_ge(sort_step, done[0])
            nc.vector.tensor_scalar(before_group, key_row, col("group_key"), None, ALU.is_lt).then_inc(sort_step, 1)
            nc.vector.reduce_sum(col("rank"), before, AX_X).then_inc(sort_step, 1)
            done[0] += 2
            dve.wait_ge(sort_step, done[0])
            link(nc.vector.reduce_sum(col("start"), before_group, AX_X))
            link(nc.vector.tensor_tensor(col("first"), col("rank"), col("start"), ALU.is_equal))
            assert done[0] == RANKED
            nc.vector.tensor_scalar(at_step, counting, col("rank"), None, ALU.is_equal).then_inc(sort_step, 1)
            nc.vector.tensor_copy(col("cond"), cond_i[:]).then_inc(sort_step, 1)
            nc.vector.tensor_scalar(col("row"), col("quad"), -float(T // B * 256 // B - NC // B), None,
                                    ALU.mult).then_inc(sort_step, 1)
            nc.vector.tensor_tensor(col("first_eye"), col("quad"), col("first"), ALU.mult).then_inc(sort_step, 1)
            done[0] += 4
            dve.wait_ge(sort_step, done[0])
            link(nc.vector.scalar_tensor_tensor(out=col("row"), in0=col("group_key"), scalar=float(T // B),
                                                in1=col("row"), op0=ALU.mult, op1=ALU.add))
            nc.vector.tensor_tensor(col("first_row"), col("row"), col("first"), ALU.mult).then_inc(sort_step, 1)
            dve.wait_ge(sort_mm, 1)
            nc.vector.tensor_scalar(col("group"), group_ps, -1.0, None, ALU.add).then_inc(sort_step, 1)
            nc.vector.tensor_copy(col("next_group"), group_ps).then_inc(sort_step, 1)
            done[0] += 3
            dve.wait_ge(sort_step, done[0])
            nc.vector.tensor_scalar(by_group[:, 0:MAXQ], counting[:, 0:MAXQ], col("group"), None,
                                    ALU.is_equal).then_inc(sort_step, 1)
            nc.vector.tensor_scalar(by_group[:, MAXQ:], counting[:, 0:MAXQ], col("next_group"), None,
                                    ALU.is_ge).then_inc(sort_step, 1)
            done[0] += 2
            assert done[0] == GROUPED
            dve.wait_ge(sort_mm, 2)
            nc.vector.tensor_copy(group_tab[:, 0:2 * MAXQ], group_tab_ps).then_inc(group_tables, 1)
            dve.wait_ge(sort_mm, 3)
            link(nc.vector.tensor_copy(step_tab[:, 0:STEPS], step_ps))
            nc.vector.tensor_scalar(buffer_tab[:], step_tab[:], 1, WBUF.bit_length() - 1, ALU.bitwise_and,
                                    ALU.logical_shift_left).then_inc(step_tables, 1)

            def add_identity(n, m, eye):
                squares = bass.AP(w_nat[m % 2], m * KP * PF, [[OA * PF, P], [PF + SQ, KP], [1, SQ]])
                one = ident[:, ds(eye, SQ)].unsqueeze(1).to_broadcast([P, KP, SQ])
                nc.vector.tensor_tensor(squares, squares, one, ALU.add).then_inc(w_diag, 1)
                dve.wait_ge(w_diag, n + 1)

            def turn(m, r0, r1):
                nat = w_nat[m % 2][:].rearrange("p (a r c) -> p r a c", r=KP, c=SQ)
                turned = w_turn[:].rearrange("p (r a c) -> p r a c", r=KP, c=SQ)
                return nc.vector.transpose(turned[:, r0:r1], nat[:, r0:r1])

            def turn_x(t):
                dve.wait_ge(x_loaded, t * (QUAD * DMA) + QUAD * DMA)
                if not (isinstance(t, int) and t == 0):
                    dve.wait_ge(x_split, t)
                nc.vector.transpose(x_turn[:].rearrange("p (k a c) -> p k a c", a=QUAD, c=SQ),
                                    x_nat[:].rearrange("p (a k c) -> p k a c", a=QUAD, c=SQ))\
                    .then_inc(x_turned, 1)

            eye = of_group(dve, EYE, 0, P - SQ)
            turn_x(0)
            for m in range(PIECES):
                dve.wait_ge(w_loaded[m % 2], (m // 2 + 1) * (QUAD * DMA))
                add_identity(m, m, eye)
                turn(m, 0, KP // 2).then_inc(w_half_turned, 1)
                turn(m, KP // 2, KP).then_inc(w_turned, 1)
                for h in range(2):
                    at = m * KP * NC + h * HALF
                    dve.wait_ge(w_rounded, 2 * m + h + 1)
                    last = nc.vector.tensor_tensor(w_low[:, at:at + HALF], w_turn[:, h * HALF:(h + 1) * HALF],
                                                   w_high[:, at:at + HALF], ALU.subtract)
                last.then_inc(w_ready, 1)
                dve.wait_ge(w_ready, m + 1)
            turn_x(1)

            def prepare(q, buf, eye, m):
                n = q * PIECES + m
                at = buf * WBUF + m * KP * NC
                high = w_high[:, at:at + KP * NC]
                low = w_low[:, at:at + KP * NC]
                dve.wait_ge(w_loaded[m % 2], (q * 2 + m // 2 + 1) * (QUAD * DMA))
                add_identity(n, m, eye)
                dve.wait_ge(w_ready, n)
                turn(m, 0, KP).then_inc(w_turned, 1)
                dve.wait_ge(w_turned, n + 3)
                nc.vector.tensor_copy(high, w_turn[:]).then_inc(w_rounded, 1)
                dve.wait_ge(w_rounded, n + PIECES + 1)
                nc.vector.tensor_tensor(low, w_turn[:], high, ALU.subtract).then_inc(w_ready, 1)

            def turn_ahead(start, end):
                with dve.If(end > start):
                    with dve.Fori(start, end) as t:
                        turn_x(t + 2)

            def beside(q, buf, first=False):
                eye = of_group(dve, EYE, q + 1, P - SQ)
                start = of_group(dve, FIRST, q + MAXQ, STEPS - 1)
                end = of_group(dve, FIRST, q + (MAXQ + 1), STEPS - 1)
                if not first:
                    dve.wait_ge(gemm_done, start + 1)
                for m in range(PIECES):
                    prepare(q + 1, buf, eye, m)
                    if m == 0:
                        turn_x(start + 2)
                    elif m < PIECES - 1:
                        with dve.If(end > start + m):
                            turn_x(start + (m + 2))
                    else:
                        turn_ahead(start + m, end)

            beside(0, 1, first=True)
            with dve.Fori(1, count_groups(dve) - 1, 2) as q:
                beside(q, 0)
                beside(q + 1, 1)
            last_start = of_group(dve, FIRST, count_groups(dve) + (MAXQ - 1), STEPS - 1)
            turn_ahead(last_start, STEPS - 1)

        @block.tensor
        def _(pe):
            pe.sem_inc(gemm_done, 1)
            pe.wait_ge(sort_step, RANKED)
            nc.tensor.matmul(group_ps, not_before, col("first"), start=True, stop=True).then_inc(sort_mm, 1)
            pe.wait_ge(sort_step, GROUPED)
            nc.tensor.matmul(group_tab_ps, col("first_row", "one"), by_group, start=True, stop=True).then_inc(sort_mm, 1)
            nc.tensor.matmul(step_ps, col("seq", "group"), at_step, start=True, stop=True).then_inc(sort_mm, 1)
            pe.wait_ge(step_tables, 1)

            def high_passes(t, s):
                q = by_step(pe, GROUP, t, MAXQ - 1)
                at = by_step(pe, GROUP, t, WBUF, buffer_tab)
                pe.wait_ge(x_high_made, t + 1)
                for k in range(KB):
                    if k % KP == 0:
                        pe.wait_ge(w_ready, q * PIECES + (k // KP + 1))
                    xs = x_high[s][:, k * P:(k + 1) * P]
                    nc.tensor.matmul(z_ps[s][:], xs, w_high[:, ds(at + k * NC, NC)], start=(k == 0), stop=False)
                    nc.tensor.matmul(z_ps[s][:], xs, w_low[:, ds(at + k * NC, NC)], start=False, stop=False)
                return at

            def low_pass(t, s, at):
                pe.wait_ge(x_split, t + 1)
                for k in range(KB):
                    xs = x_low[s][:, k * P:(k + 1) * P]
                    last = nc.tensor.matmul(z_ps[s][:], xs, w_high[:, ds(at + k * NC, NC)],
                                            start=False, stop=(k == KB - 1))
                last.then_inc(gemm_done, 1)

            def by_a(t):
                pe.wait_ge(z_split, t + 1)
                pe.wait_ge(a_split, t + 1)
                pe.wait_ge(out_copied, t + 1)
                nc.tensor.matmul(out_ps[:], a_high[:], z_high[:], start=True, stop=False)
                nc.tensor.matmul(out_ps[:], a_high[:], z_low[:], start=False, stop=False)
                nc.tensor.matmul(out_ps[:], a_low[:], z_high[:], start=False, stop=True).then_inc(out_made, 1)

            def step(t, s):
                at = high_passes(t, s)
                by_a(t - 1)
                low_pass(t, s, at)

            low_pass(0, 0, high_passes(0, 0))
            with nc.Fori(0, STEPS // 2 - 1, engines=(mybir.EngineType.PE,), hint_back_edge=True) as p:
                step(2 * p + 1, 1)
                step(2 * p + 2, 0)
            step(STEPS - 1, 1)
            by_a(STEPS - 1)


RANKED = 19
GROUPED = 29


_INS = ["x", "itok_B_0_15", "itok_B_3_7", "L0_cond_weights", "L1_cond_weight"]


def kernel(**inputs):
    import numpy as np
    import concourse.bacc as bacc
    from concourse.bass_utils import run_bass_kernel_spmd

    nc = bacc.Bacc("TRN2", target_bir_lowering=False, num_devices=1, dynamic_dma_scratch_size=1024)
    arrays, args = {}, []
    for name in _INS:
        a = np.ascontiguousarray(inputs[name])
        arrays[f"in_{name}"] = a
        args.append(nc.dram_tensor(f"in_{name}", a.shape, mybir.dt.from_np(a.dtype), kind="ExternalInput").ap())
    args.append(nc.dram_tensor("out", (B, P, T), F32, kind="ExternalOutput").ap())
    build(nc, *args)
    r = run_bass_kernel_spmd(nc, [arrays], core_ids=[0])
    return r.results[0]["out"]
```

```python
from contextlib import ExitStack

import concourse.bass as bass
from concourse import mybir

F32 = mybir.dt.float32
F32R = mybir.dt.float32r
I32 = mybir.dt.int32
ALU = mybir.AluOpType
COPY = mybir.ActivationFunctionType.Copy
AX_X = mybir.AxisListType.X
ds = bass.ds

P = 128
B = 32
T = 2048
NC = 512
CHUNKS = T // NC
STEPS = CHUNKS * B
KB = T // P
SQ = 32
QUAD = P // SQ
PIECES = 4
KP = KB // PIECES
PF = SQ * KP
XF = T // QUAD
OA = NC // SQ
WBUF = KB * NC
HALF = KP * NC // 2
HELPED = (1, 2)
MAXQ = 32
DMA = 16


def build(nc, x, cond, adapter, w0, w1, out):
    ctx = ExitStack()
    with ctx:
        def sb(name, shape, dt=F32):
            return ctx.enter_context(nc.sbuf_tensor(name, shape, dt))

        def ps(name, shape):
            return ctx.enter_context(nc.psum_tensor(name, shape, F32))

        def sem(name):
            return ctx.enter_context(nc.semaphore(name))

        w_high = sb("w_high", [P, 2 * WBUF], F32R)
        w_low = sb("w_low", [P, 2 * WBUF], F32R)
        w_nat = [sb(f"w_nat{s}", [P, OA * PF]) for s in range(2)]
        w_turn = [sb(f"w_turn{s}", [P, KP * NC]) for s in range(2)]
        x_nat = sb("x_nat", [P, QUAD * XF])
        x_turn = sb("x_turn", [P, KB * P])
        x_high = [sb(f"x_high{s}", [P, KB * P], F32R) for s in range(2)]
        x_low = [sb(f"x_low{s}", [P, KB * P], F32R) for s in range(2)]
        z_raw = sb("z_raw", [P, NC])
        z_high = sb("z_high", [P, NC], F32R)
        z_low = sb("z_low", [P, NC], F32R)
        a_full = sb("a_full", [P, P])
        a_high = sb("a_high", [P, P], F32R)
        a_low = sb("a_low", [P, P], F32R)
        out_sb = [sb(f"out_sb{s}", [P, NC]) for s in range(2)]
        ident = sb("ident", [P, P])

        chunk_seq, counting, key_row, not_before, at_step, own, before, before_group, hot = (
            x_turn[:, i * P:(i + 1) * P] for i in range(9))
        by_group = hot[:, 0:2 * MAXQ]
        part_i = sb("part_i", [P, 1], I32)
        seq_i = sb("seq_i", [P, 1], I32)
        quad_i = sb("quad_i", [P, 1], I32)
        ids_row = sb("ids_row", [P, B], I32)
        cond_i = sb("cond_i", [P, 1], I32)
        cols = sb("cols", [P, 15])
        COLS = ["seq", "cond", "result", "group", "first_row", "first_eye", "one",
                "quad", "key", "group_key", "rank", "start", "first", "row", "next_group"]

        def col(first, last=None):
            return cols[:, COLS.index(first):COLS.index(last or first) + 1]
        SEQ, COND, RESULT, GROUP = range(4)
        step_tab = sb("step_tab", [4, STEPS + 2], I32)
        buffer_tab = sb("buffer_tab", [4, STEPS + 2], I32)
        ROW, EYE, FIRST = range(3)
        group_tab = sb("group_tab", [3, 2 * MAXQ + 2], I32)

        first_key = sb("first_key", [1, 1], I32)
        first_tab = sb("first_tab", [1, 2], I32)

        z_ps = [ps(f"z_ps{s}", [P, NC]) for s in range(2)]
        out_ps = ps("out_ps", [P, NC])
        group_ps, group_tab_ps, step_ps = z_ps[1][:, 0:1], z_ps[1][0:3, P:P + 2 * MAXQ], z_ps[0][0:4, 0:STEPS]

        ids_loaded = sem("ids_loaded")
        consts_made = sem("consts_made")
        sort_step = sem("sort_step")
        sort_mm = sem("sort_mm")
        first_known = sem("first_known")
        tables_made = sem("tables_made")
        w_loaded = [sem(f"w_loaded{s}") for s in range(2)]
        w_diag = sem("w_diag")
        w_half_turned = sem("w_half_turned")
        w_turned = sem("w_turned")
        w_rounded = sem("w_rounded")
        w_ready = sem("w_ready")
        w_helped = sem("w_helped")
        x_loaded = sem("x_loaded")
        x_turned = sem("x_turned")
        x_high_made = sem("x_high_made")
        x_split = sem("x_split")
        a_loaded = sem("a_loaded")
        a_ready = sem("a_ready")
        a_high_made = sem("a_high_made")
        a_split = sem("a_split")
        gemm_done = sem("gemm_done")
        z_copied = sem("z_copied")
        z_split = sem("z_split")
        out_made = sem("out_made")
        out_copied = sem("out_copied")
        out_stored = [sem(f"out_stored{s}") for s in range(2)]

        block = ctx.enter_context(nc.Block())

        def by_step(eng, row, t, most, tab=step_tab):
            return eng.value_load(tab[row:row + 1, ds(t, 1)], min_val=0, max_val=most)

        def of_group(eng, row, q, most):
            return eng.value_load(group_tab[row:row + 1, ds(q, 1)], min_val=0, max_val=most)

        def count_groups(eng):
            return by_step(eng, GROUP, STEPS - 1, MAXQ - 1) + 1

        def load_sequence(eng, b):
            for j in range(QUAD):
                eng.dma_start(x_nat[j * SQ:(j + 1) * SQ, :].rearrange("p (a f) -> p a f", a=QUAD),
                              x[ds(b, 1), :, j * XF:(j + 1) * XF].rearrange("o (a p) f -> p (o a) f", p=SQ))\
                    .then_inc(x_loaded, DMA)

        @block.sync
        def _(sp):
            sp.dma_start(ids_row[:], adapter.partition_broadcast(P)).then_inc(ids_loaded, DMA)
            sp.dma_start(cond_i[:], bass.AP(cond.tensor, 0, [[0, CHUNKS], [1, B], [1, 1]])).then_inc(ids_loaded, DMA)
            sp.wait_ge(first_known, 2)
            rows = w1.rearrange("e o i -> (e o) i")

            def load_group(q, row):
                chunk = rows[ds(row, NC), :].rearrange("(a p) i -> p a i", p=SQ)
                for m in range(PIECES):
                    s = m % 2
                    sp.wait_ge(w_turned, q * PIECES + m + 1)
                    for b in range(QUAD):
                        i0 = b * (T // QUAD) + m * PF
                        sp.dma_start(w_nat[s][b * SQ:(b + 1) * SQ, :].rearrange("p (a f) -> p a f", f=PF),
                                     chunk[:, :, i0:i0 + PF]).then_inc(w_loaded[s], DMA)

            load_sequence(sp, sp.value_load(first_tab[:, 0:1], min_val=0, max_val=B - 1))
            load_group(0, sp.value_load(first_tab[:, 1:2], min_val=0, max_val=rows.shape[0] - NC))
            sp.wait_ge(tables_made, 2)
            with sp.Fori(1, count_groups(sp)) as q:
                load_group(q, of_group(sp, ROW, q, rows.shape[0] - NC))

        @block.gpsimd
        def _(pool):
            nc.gpsimd.memset(ident[:], 0.0).then_inc(consts_made, 1)
            nc.gpsimd.iota(chunk_seq.rearrange("p (c b) -> p c b", b=B), [[256, CHUNKS], [1, B]], channel_multiplier=0,
                           allow_small_or_imprecise_dtypes=True).then_inc(consts_made, 1)
            nc.gpsimd.iota(counting, [[1, P]], channel_multiplier=0,
                           allow_small_or_imprecise_dtypes=True).then_inc(consts_made, 1)
            nc.gpsimd.iota(part_i[:], [[0, 1]], channel_multiplier=1).then_inc(consts_made, 1)
            pool.wait_ge(consts_made, 1)
            nc.gpsimd.affine_select(out=ident[:], in_=ident[:], compare_op=ALU.not_equal, fill=1.0, base=0,
                                    pattern=[[-1, P]], channel_multiplier=1).then_inc(consts_made, 1)
            pool.wait_ge(consts_made, 5)

            def x_rest(t, s):
                for h in range(2):
                    half = slice(h * T // 2, (h + 1) * T // 2)
                    pool.wait_ge(x_high_made, t * 2 + (h + 1))
                    nc.gpsimd.tensor_tensor(x_low[s][:, half], x_turn[:, half], x_high[s][:, half], ALU.subtract)\
                        .then_inc(x_split, 1)

            def z_rest(t):
                pool.wait_ge(z_copied, 2 * t + 2)
                nc.gpsimd.tensor_tensor(z_low[:], z_raw[:], z_high[:], ALU.subtract).then_inc(z_split, 1)

            def a_parts(t):
                pool.wait_ge(a_loaded, (t + 1) * DMA)
                nc.gpsimd.tensor_tensor(a_full[:], a_full[:], ident[:], ALU.add).then_inc(a_ready, 1)
                pool.wait_ge(a_high_made, t + 1)
                nc.gpsimd.tensor_tensor(a_low[:], a_full[:], a_high[:], ALU.subtract).then_inc(a_split, 1)

            x_rest(0, 0)
            for m in HELPED:
                at = m * KP * NC + HALF
                pool.wait_ge(w_rounded, 2 * m + 2)
                nc.gpsimd.tensor_tensor(w_low[:, at:at + HALF], w_turn[m % 2][:, HALF:2 * HALF], w_high[:, at:at + HALF],
                                        ALU.subtract).then_inc(w_helped, 1)
            x_rest(1, 1)
            a_parts(0)
            with pool.Fori(0, STEPS // 2 - 1) as p:
                for s in (1, 0):
                    t = 2 * p + (2 - s)
                    z_rest(t - 1)
                    x_rest(t + 1, 1 - s)
                    a_parts(t)
            z_rest(STEPS - 2)
            a_parts(STEPS - 1)

        @block.scalar
        def _(act):
            act.sem_inc(out_copied, 1)

            def load_x(t):
                load_sequence(act, by_step(act, SEQ, t, B - 1))

            def load_a(t):
                c = by_step(act, COND, t, w0.shape[0] - 1)
                act.dma_start(a_full[:], w0[ds(c, 1), :, :].rearrange("o c d -> (o c) d")).then_inc(a_loaded, DMA)

            def take_x(t, s):
                for h in range(2):
                    half = slice(h * T // 2, (h + 1) * T // 2)
                    act.wait_ge(x_turned, t * 2 + (h + 1))
                    nc.scalar.activation(x_high[s][:, half], x_turn[:, half], COPY).then_inc(x_high_made, 1)

            def take_z(t, s, raw=True):
                act.wait_ge(gemm_done, t + 2)
                if raw:
                    nc.scalar.activation(z_raw[:], z_ps[s][:], COPY).then_inc(z_copied, 1)
                nc.scalar.activation(z_high[:], z_ps[s][:], COPY).then_inc(z_copied, 1)

            def take_out(t, s, stored):
                at = by_step(act, RESULT, t, B * P * T - NC)
                if stored is not None:
                    act.wait_ge(out_stored[s], stored * DMA)
                act.wait_ge(out_made, t + 1)
                nc.scalar.activation(out_sb[s][:], out_ps[:], COPY).then_inc(out_copied, 1)
                act.wait_ge(out_copied, t + 2)
                act.dma_start(bass.AP(out.tensor, at, [[T, P], [1, NC]]), out_sb[s][:]).then_inc(out_stored[s], DMA)

            def take_a(t):
                act.wait_ge(a_ready, t + 1)
                nc.scalar.activation(a_high[:], a_full[:], COPY).then_inc(a_high_made, 1)

            def beside(t, s, stored, more=True):
                take_z(t - 1, 1 - s)
                if more:
                    take_x(t + 1, 1 - s)
                    load_x(t + 2)
                act.wait_ge(a_split, t)
                load_a(t)
                take_out(t - 1, 1 - s, stored)
                take_a(t)

            act.wait_ge(consts_made, 5)
            nc.scalar.activation(out_sb[0][:, 0:1], ident[:, 0:1], COPY)

            act.wait_ge(tables_made, 2)
            load_a(0)
            take_x(0, 0)
            for m in range(PIECES):
                for h in range(2):
                    if h == 0:
                        act.wait_ge(w_half_turned, m + 1)
                    else:
                        act.wait_ge(w_turned, m + 3)
                    at = m * KP * NC + h * HALF
                    nc.scalar.activation(w_high[:, at:at + HALF], w_turn[m % 2][:, h * HALF:(h + 1) * HALF], COPY)\
                        .then_inc(w_rounded, 1)
                if m == 0:
                    load_x(1)
            take_x(1, 1)
            load_x(2)
            take_a(0)

            beside(1, 1, None)
            beside(2, 0, None)
            with act.Fori(1, STEPS // 2 - 1) as p:
                beside(2 * p + 1, 1, p)
                beside(2 * p + 2, 0, p)
            beside(STEPS - 1, 1, STEPS // 2 - 1, more=False)
            take_z(STEPS - 1, 1, raw=False)
            take_out(STEPS - 1, 1, STEPS // 2 - 1)
            for s in range(2):
                act.wait_ge(out_stored[s], STEPS // 2 * DMA)

        @block.vector
        def _(dve):
            done = [0]

            def link(instruction):
                done[0] += 1
                instruction.then_inc(sort_step, 1)
                dve.wait_ge(sort_step, done[0])

            dve.sem_inc(w_turned, 2)
            nc.vector.memset(cols[:], 0.0).then_inc(sort_step, 1)
            nc.vector.memset(step_tab[:], 0).then_inc(sort_step, 1)
            done[0] = 2
            dve.wait_ge(consts_made, 5)
            nc.vector.tensor_scalar(seq_i[:], part_i[:], B - 1, None, ALU.bitwise_and).then_inc(sort_step, 1)
            nc.vector.tensor_scalar(quad_i[:], part_i[:], P - B, None, ALU.bitwise_and).then_inc(sort_step, 1)
            done[0] += 2
            dve.wait_ge(sort_step, done[0])
            nc.vector.tensor_copy(col("seq"), seq_i[:]).then_inc(sort_step, 1)
            nc.vector.tensor_copy(col("quad"), quad_i[:]).then_inc(sort_step, 1)
            nc.vector.tensor_scalar(col("result"), quad_i[:], float(NC // B), None, ALU.mult).then_inc(sort_step, 1)
            nc.vector.memset(col("one"), 1.0).then_inc(sort_step, 1)
            done[0] += 4
            dve.wait_ge(sort_step, done[0])
            link(nc.vector.scalar_tensor_tensor(out=col("result"), in0=col("seq"), scalar=float(P * T),
                                                in1=col("result"), op0=ALU.mult, op1=ALU.add))
            dve.wait_ge(ids_loaded, 2 * DMA)
            link(nc.vector.scalar_tensor_tensor(
                out=key_row.rearrange("p (c b) -> p c b", b=B),
                in0=ids_row[:].unsqueeze(1).to_broadcast([P, CHUNKS, B]), scalar=float(B),
                in1=chunk_seq.rearrange("p (c b) -> p c b", b=B), op0=ALU.mult, op1=ALU.add))
            link(nc.vector.tensor_reduce(first_key[:], key_row[0:1, 0:B], AX_X, ALU.min))
            nc.vector.tensor_scalar(first_tab[:, 0:1], first_key[:], B - 1, None, ALU.bitwise_and)\
                .then_inc(first_known, 1)
            nc.vector.tensor_scalar(first_tab[:, 1:2], first_key[:], 256 - B, (T // B).bit_length() - 1, ALU.bitwise_and,
                                    ALU.logical_shift_left).then_inc(first_known, 1)
            link(nc.vector.tensor_tensor(own, key_row, ident[:], ALU.mult))
            link(nc.vector.reduce_sum(col("key"), own, AX_X))
            nc.vector.tensor_scalar(before, key_row, col("key"), None, ALU.is_lt).then_inc(sort_step, 1)
            nc.vector.tensor_tensor(col("group_key"), col("key"), col("seq"), ALU.subtract).then_inc(sort_step, 1)
            nc.vector.tensor_scalar(not_before, key_row, col("key"), None, ALU.is_ge).then_inc(sort_step, 1)
            done[0] += 3
            dve.wait_ge(sort_step, done[0])
            nc.vector.tensor_scalar(before_group, key_row, col("group_key"), None, ALU.is_lt).then_inc(sort_step, 1)
            nc.vector.reduce_sum(col("rank"), before, AX_X).then_inc(sort_step, 1)
            done[0] += 2
            dve.wait_ge(sort_step, done[0])
            link(nc.vector.reduce_sum(col("start"), before_group, AX_X))
            link(nc.vector.tensor_tensor(col("first"), col("rank"), col("start"), ALU.is_equal))
            assert done[0] == RANKED
            nc.vector.tensor_scalar(at_step, counting, col("rank"), None, ALU.is_equal).then_inc(sort_step, 1)
            nc.vector.tensor_copy(col("cond"), cond_i[:]).then_inc(sort_step, 1)
            nc.vector.tensor_scalar(col("row"), col("quad"), -float(T // B * 256 // B - NC // B), None,
                                    ALU.mult).then_inc(sort_step, 1)
            nc.vector.tensor_tensor(col("first_eye"), col("quad"), col("first"), ALU.mult).then_inc(sort_step, 1)
            done[0] += 4
            dve.wait_ge(sort_step, done[0])
            link(nc.vector.scalar_tensor_tensor(out=col("row"), in0=col("group_key"), scalar=float(T // B),
                                                in1=col("row"), op0=ALU.mult, op1=ALU.add))
            nc.vector.tensor_tensor(col("first_row"), col("row"), col("first"), ALU.mult).then_inc(sort_step, 1)
            dve.wait_ge(sort_mm, 1)
            nc.vector.tensor_scalar(col("group"), group_ps, -1.0, None, ALU.add).then_inc(sort_step, 1)
            nc.vector.tensor_copy(col("next_group"), group_ps).then_inc(sort_step, 1)
            done[0] += 3
            dve.wait_ge(sort_step, done[0])
            nc.vector.tensor_scalar(by_group[:, 0:MAXQ], counting[:, 0:MAXQ], col("group"), None,
                                    ALU.is_equal).then_inc(sort_step, 1)
            nc.vector.tensor_scalar(by_group[:, MAXQ:], counting[:, 0:MAXQ], col("next_group"), None,
                                    ALU.is_ge).then_inc(sort_step, 1)
            done[0] += 2
            assert done[0] == GROUPED
            dve.wait_ge(sort_mm, 2)
            nc.vector.tensor_copy(group_tab[:, 0:2 * MAXQ], group_tab_ps).then_inc(tables_made, 1)
            dve.wait_ge(sort_mm, 3)
            link(nc.vector.tensor_copy(step_tab[:, 0:STEPS], step_ps))
            nc.vector.tensor_scalar(buffer_tab[:], step_tab[:], 1, WBUF.bit_length() - 1, ALU.bitwise_and,
                                    ALU.logical_shift_left).then_inc(tables_made, 1)

            def add_identity(n, m, eye):
                squares = bass.AP(w_nat[m % 2], m * KP * PF, [[OA * PF, P], [PF + SQ, KP], [1, SQ]])
                one = ident[:, ds(eye, SQ)].unsqueeze(1).to_broadcast([P, KP, SQ])
                nc.vector.tensor_tensor(squares, squares, one, ALU.add).then_inc(w_diag, 1)
                dve.wait_ge(w_diag, n + 1)

            def turn(m, r0, r1):
                nat = w_nat[m % 2][:].rearrange("p (a r c) -> p r a c", r=KP, c=SQ)
                turned = w_turn[m % 2][:].rearrange("p (r a c) -> p r a c", r=KP, c=SQ)
                return nc.vector.transpose(turned[:, r0:r1], nat[:, r0:r1])

            def turn_x(t, ahead):
                dve.wait_ge(x_loaded, t * (QUAD * DMA) + (ahead + 1) * (QUAD * DMA))
                for h in range(2):
                    blocks = slice(h * KB // 2, (h + 1) * KB // 2)
                    if ahead > 0:
                        dve.wait_ge(x_split, t * 2 + (2 * ahead - 1 + h))
                    nc.vector.transpose(x_turn[:].rearrange("p (k a c) -> p k a c", a=QUAD, c=SQ)[:, blocks],
                                        x_nat[:].rearrange("p (a k c) -> p k a c", a=QUAD, c=SQ)[:, blocks])\
                        .then_inc(x_turned, 1)

            turn_x(0, 0)
            for m in range(PIECES):
                dve.wait_ge(w_loaded[m % 2], (m // 2 + 1) * (QUAD * DMA))
                add_identity(m, m, 0)
                if m >= 2:
                    dve.wait_ge(w_ready, m - 1)
                if m - 2 in HELPED:
                    dve.wait_ge(w_helped, HELPED.index(m - 2) + 1)
                turn(m, 0, KP // 2).then_inc(w_half_turned, 1)
                turn(m, KP // 2, KP).then_inc(w_turned, 1)
                for h in range(1 if m in HELPED else 2):
                    at = m * KP * NC + h * HALF
                    dve.wait_ge(w_rounded, 2 * m + h + 1)
                    last = nc.vector.tensor_tensor(w_low[:, at:at + HALF], w_turn[m % 2][:, h * HALF:(h + 1) * HALF],
                                                   w_high[:, at:at + HALF], ALU.subtract)
                last.then_inc(w_ready, 1)
            turn_x(0, 1)
            dve.wait_ge(w_helped, len(HELPED))

            def prepare(q, buf, eye, m):
                n = q * PIECES + m
                at = buf * WBUF + m * KP * NC
                high = w_high[:, at:at + KP * NC]
                low = w_low[:, at:at + KP * NC]
                dve.wait_ge(w_loaded[m % 2], (q * 2 + m // 2 + 1) * (QUAD * DMA))
                add_identity(n, m, eye)
                dve.wait_ge(w_ready, n - 1)
                turn(m, 0, KP).then_inc(w_turned, 1)
                dve.wait_ge(w_turned, n + 3)
                nc.vector.tensor_copy(high, w_turn[m % 2][:]).then_inc(w_rounded, 1)
                dve.wait_ge(w_rounded, n + PIECES + 1)
                nc.vector.tensor_tensor(low, w_turn[m % 2][:], high, ALU.subtract).then_inc(w_ready, 1)

            def turn_ahead(start, end):
                with dve.If(end > start):
                    with dve.Fori(start, end) as t:
                        turn_x(t, 2)

            def beside(q, buf, first=False):
                eye = of_group(dve, EYE, q + 1, P - SQ)
                start = of_group(dve, FIRST, q + MAXQ, STEPS - 1)
                end = of_group(dve, FIRST, q + (MAXQ + 1), STEPS - 1)
                if not first:
                    dve.wait_ge(gemm_done, start + 1)
                for m in range(PIECES):
                    prepare(q + 1, buf, eye, m)
                    if m == 0:
                        turn_x(start, 2)
                    elif m < PIECES - 1:
                        with dve.If(end > start + m):
                            turn_x(start, m + 2)
                    else:
                        turn_ahead(start + m, end)

            beside(0, 1, first=True)
            with dve.Fori(1, count_groups(dve) - 1, 2) as q:
                beside(q, 0)
                beside(q + 1, 1)
            last_start = of_group(dve, FIRST, count_groups(dve) + (MAXQ - 1), STEPS - 1)
            turn_ahead(last_start, STEPS - 1)
            dve.wait_ge(z_copied, 2 * STEPS - 1)
            nc.vector.tensor_tensor(z_low[:], z_ps[1][:], z_high[:], ALU.subtract).then_inc(z_split, 1)

        @block.tensor
        def _(pe):
            pe.sem_inc(gemm_done, 1)
            pe.wait_ge(sort_step, RANKED)
            nc.tensor.matmul(group_ps, not_before, col("first"), start=True, stop=True).then_inc(sort_mm, 1)
            pe.wait_ge(sort_step, GROUPED)
            nc.tensor.matmul(group_tab_ps, col("first_row", "one"), by_group, start=True, stop=True).then_inc(sort_mm, 1)
            nc.tensor.matmul(step_ps, col("seq", "group"), at_step, start=True, stop=True).then_inc(sort_mm, 1)
            pe.wait_ge(tables_made, 2)

            def high_passes(t, s):
                q = by_step(pe, GROUP, t, MAXQ - 1)
                at = by_step(pe, GROUP, t, WBUF, buffer_tab)
                for k in range(KB):
                    if k % (KB // 2) == 0:
                        pe.wait_ge(x_high_made, t * 2 + (1 + 2 * k // KB))
                    if k % KP == 0:
                        pe.wait_ge(w_ready, q * PIECES + (k // KP + 1))
                    xs = x_high[s][:, k * P:(k + 1) * P]
                    nc.tensor.matmul(z_ps[s][:], xs, w_high[:, ds(at + k * NC, NC)], start=(k == 0), stop=False)
                    nc.tensor.matmul(z_ps[s][:], xs, w_low[:, ds(at + k * NC, NC)], start=False, stop=False)
                return at

            def low_pass(t, s, at):
                for k in range(KB):
                    if k % (KB // 2) == 0:
                        pe.wait_ge(x_split, t * 2 + (1 + 2 * k // KB))
                    xs = x_low[s][:, k * P:(k + 1) * P]
                    last = nc.tensor.matmul(z_ps[s][:], xs, w_high[:, ds(at + k * NC, NC)],
                                            start=False, stop=(k == KB - 1))
                last.then_inc(gemm_done, 1)

            def by_a(t, copies):
                pe.wait_ge(z_copied, copies)
                pe.wait_ge(a_split, t + 1)
                pe.wait_ge(out_copied, t + 1)
                nc.tensor.matmul(out_ps[:], a_high[:], z_high[:], start=True, stop=False)
                nc.tensor.matmul(out_ps[:], a_low[:], z_high[:], start=False, stop=False)
                pe.wait_ge(z_split, t + 1)
                nc.tensor.matmul(out_ps[:], a_high[:], z_low[:], start=False, stop=True).then_inc(out_made, 1)

            def step(t, s):
                at = high_passes(t, s)
                by_a(t - 1, t * 2)
                low_pass(t, s, at)

            for k in range(KB):
                if k % (KB // 2) == 0:
                    pe.wait_ge(x_high_made, 1 + 2 * k // KB)
                    pe.wait_ge(x_split, 1 + 2 * k // KB)
                if k % KP == 0:
                    pe.wait_ge(w_ready, k // KP + 1)
                    if k // KP in HELPED:
                        pe.wait_ge(w_helped, HELPED.index(k // KP) + 1)
                xs = x_high[0][:, k * P:(k + 1) * P]
                w_block = slice(k * NC, (k + 1) * NC)
                nc.tensor.matmul(z_ps[0][:], xs, w_high[:, w_block], start=(k == 0), stop=False)
                nc.tensor.matmul(z_ps[0][:], xs, w_low[:, w_block], start=False, stop=False)
                last = nc.tensor.matmul(z_ps[0][:], x_low[0][:, k * P:(k + 1) * P], w_high[:, w_block],
                                        start=False, stop=(k == KB - 1))
            last.then_inc(gemm_done, 1)
            with nc.Fori(0, STEPS // 2 - 1, engines=(mybir.EngineType.PE,), hint_back_edge=True) as p:
                step(2 * p + 1, 1)
                step(2 * p + 2, 0)
            step(STEPS - 1, 1)
            by_a(STEPS - 1, 2 * STEPS - 1)


RANKED = 20
GROUPED = 30


_INS = ["x", "itok_B_0_15", "itok_B_3_7", "L0_cond_weights", "L1_cond_weight"]


def kernel(**inputs):
    import numpy as np
    import concourse.bacc as bacc
    from concourse.bass_utils import run_bass_kernel_spmd

    nc = bacc.Bacc("TRN2", target_bir_lowering=False, num_devices=1, dynamic_dma_scratch_size=1024)
    arrays, args = {}, []
    for name in _INS:
        a = np.ascontiguousarray(inputs[name])
        arrays[f"in_{name}"] = a
        args.append(nc.dram_tensor(f"in_{name}", a.shape, mybir.dt.from_np(a.dtype), kind="ExternalInput").ap())
    args.append(nc.dram_tensor("out", (B, P, T), F32, kind="ExternalOutput").ap())
    build(nc, *args)
    r = run_bass_kernel_spmd(nc, [arrays], core_ids=[0])
    return r.results[0]["out"]
```
